# Optimizing a Trainium2 kernel written in Bass

```python
import numpy as np
import jax
import jax.numpy as jnp

def _softmax(x, axis=-1):
    return jax.nn.softmax(x, axis=axis)

def _gelu(x):
    return jax.nn.gelu(x, approximate=True)

def _silu(x):
    return jax.nn.silu(x)

def _sigmoid(x):
    return jax.nn.sigmoid(x)

def _layernorm(x, axis=-1, eps=1e-05):
    m = jnp.mean(x, axis=axis, keepdims=True)
    v = jnp.var(x, axis=axis, keepdims=True)
    return (x - m) / jnp.sqrt(v + eps)

def _scatter_add(tgt, idx, src, axis=0):
    return tgt.at[idx].add(src)

def _segment_sum(src, seg, n):
    return jax.ops.segment_sum(src, seg, n)
kernel_name = 'mk_adj_resnorm_d2_adj_r2_60ac0c'

def setup_inputs(seed: int=0):
    np.random.seed(seed)
    _w = jnp.asarray

    def _rec_inputs():
        import jax
        import jax.numpy as jnp
        _gk = jax.random.key(seed)
        x = -0.000929 + 1 * jax.random.normal(jax.random.fold_in(_gk, 1), (4096, 128), jnp.float32)
        _a = jax.random.bernoulli(jax.random.fold_in(_gk, 2), 0.00195312, (4096, 4096))
        _af = _a.astype(jnp.float32)
        adj = _af
        return (x, adj)
    x, adj = _rec_inputs()

    def _L0_gnn_setup():
        import jax, jax.numpy as jnp
        import numpy as np
        N, IN_DIM, OUT_DIM, HEADS = (2048, 128, 128, 4)
        D_K = OUT_DIM // HEADS
        NEG_SLOPE = 0.2
        key = jax.random.key(seed)
        k1, k2, k3, k4, k5 = jax.random.split(key, 5)
        H = jax.random.normal(k1, (N, IN_DIM), dtype=jnp.float32)
        A = jax.random.randint(k2, (N, N), 0, 2).astype(jnp.float32)
        W = jax.random.normal(k3, (OUT_DIM, IN_DIM), dtype=jnp.float32) * (1.0 / np.sqrt(IN_DIM))
        a_l = jax.random.normal(k4, (HEADS, D_K), dtype=jnp.float32) * 0.1
        a_r = jax.random.normal(k5, (HEADS, D_K), dtype=jnp.float32) * 0.1
        return {'H': H, 'A': A, 'W': W, 'a_l': a_l, 'a_r': a_r}
    _L0_gnn_all = _L0_gnn_setup()
    _L0_gnn_in = {k: v for k, v in _L0_gnn_all.items() if k in ('W', 'a_l', 'a_r')}
    del _L0_gnn_all

    def _L1_gnn_setup():
        import jax, jax.numpy as jnp
        import numpy as np
        D_IN = 128
        D_ATTN = 64
        STEPS = 2
        TOP_P = 0.9
        TAU = 1.0
        LN_EPS = 1e-05
        N_NODES = 4096

        def _top_p_attention(X, W1, W2, W3):
            q = X @ W1.T @ W2.T
            k = X @ W3.T
            logits = q @ k.T / TAU
            probs = jax.nn.softmax(logits, axis=-1)
            idx = jnp.argsort(-probs, axis=-1)
            sp = jnp.take_along_axis(probs, idx, axis=-1)
            cs = jnp.cumsum(sp, axis=-1)
            keep_sorted = cs - sp < TOP_P
            rows = jnp.arange(probs.shape[0])[:, None]
            mask = jnp.zeros(probs.shape, dtype=bool).at[rows, idx].set(keep_sorted)
            A = probs * mask
            return A / jnp.maximum(A.sum(-1, keepdims=True), 1e-12)
        key = jax.random.key(seed)
        ks = jax.random.split(key, 8)
        N, d, da, steps = (N_NODES, D_IN, D_ATTN, STEPS)
        X = jax.random.normal(ks[0], (N, d), dtype=jnp.float32)
        S = jax.random.uniform(ks[1], (N, N), dtype=jnp.float32)
        W1 = jax.random.normal(ks[2], (da, d), dtype=jnp.float32) / np.sqrt(d)
        W2 = jax.random.normal(ks[3], (da, da), dtype=jnp.float32) / np.sqrt(da)
        W3 = jax.random.normal(ks[4], (da, d), dtype=jnp.float32) / np.sqrt(d)
        U1 = jax.random.normal(ks[5], (steps, d, d), dtype=jnp.float32) / np.sqrt(d)
        U2 = jax.random.normal(ks[6], (steps, d, d), dtype=jnp.float32) / np.sqrt(d)
        ln_g = jnp.ones((d,), dtype=jnp.float32)
        ln_b = jnp.zeros((d,), dtype=jnp.float32)
        return {'X': X, 'S': S, 'W1': W1, 'W2': W2, 'W3': W3, 'U1': U1, 'U2': U2, 'ln_g': ln_g, 'ln_b': ln_b}
    _L1_gnn_all = _L1_gnn_setup()
    _L1_gnn_in = {k: v for k, v in _L1_gnn_all.items() if k in ('W1', 'W2', 'W3', 'U1', 'U2', 'ln_g', 'ln_b')}
    del _L1_gnn_all
    return {'x': x, 'adj': adj, 'L0_gnn_W': _L0_gnn_in['W'], 'L0_gnn_a_l': _L0_gnn_in['a_l'], 'L0_gnn_a_r': _L0_gnn_in['a_r'], 'L1_gnn_W1': _L1_gnn_in['W1'], 'L1_gnn_W2': _L1_gnn_in['W2'], 'L1_gnn_W3': _L1_gnn_in['W3'], 'L1_gnn_U1': _L1_gnn_in['U1'], 'L1_gnn_U2': _L1_gnn_in['U2'], 'L1_gnn_ln_g': _L1_gnn_in['ln_g'], 'L1_gnn_ln_b': _L1_gnn_in['ln_b']}

def reference(x, adj, L0_gnn_W, L0_gnn_a_l, L0_gnn_a_r, L1_gnn_W1, L1_gnn_W2, L1_gnn_W3, L1_gnn_U1, L1_gnn_U2, L1_gnn_ln_g, L1_gnn_ln_b):
    import jax
    import jax.numpy as jnp

    def _L0_gnn_ref(H, A, W, a_l, a_r):
        import jax, jax.numpy as jnp
        import numpy as np
        N, IN_DIM, OUT_DIM, HEADS = (2048, 128, 128, 4)
        D_K = OUT_DIM // HEADS
        NEG_SLOPE = 0.2
        n = H.shape[0]
        A_tilde = A + jnp.eye(n, dtype=A.dtype)
        mask = A_tilde > 0
        Wh = (H @ W.T).reshape(n, HEADS, D_K)
        score_l = jnp.einsum('nhd,hd->nh', Wh, a_l)
        score_r = jnp.einsum('nhd,hd->nh', Wh, a_r)
        e = score_l[:, :, None] + score_r.T[None, :, :]
        e = jnp.where(e >= 0, e, NEG_SLOPE * e)
        e = jnp.where(mask[:, None, :], e, -jnp.inf)
        alpha = jax.nn.softmax(e, axis=2)
        out = jnp.einsum('nhm,mhd->nhd', alpha, Wh).reshape(n, OUT_DIM)
        return jax.nn.elu(out)

    def _L1_gnn_ref(X, S, W1, W2, W3, U1, U2, ln_g, ln_b):
        import jax, jax.numpy as jnp
        import numpy as np
        D_IN = 128
        D_ATTN = 64
        STEPS = 2
        TOP_P = 0.9
        TAU = 1.0
        LN_EPS = 1e-05
        N_NODES = 4096

        def _top_p_attention(X, W1, W2, W3):
            q = X @ W1.T @ W2.T
            k = X @ W3.T
            logits = q @ k.T / TAU
            probs = jax.nn.softmax(logits, axis=-1)
            idx = jnp.argsort(-probs, axis=-1)
            sp = jnp.take_along_axis(probs, idx, axis=-1)
            cs = jnp.cumsum(sp, axis=-1)
            keep_sorted = cs - sp < TOP_P
            rows = jnp.arange(probs.shape[0])[:, None]
            mask = jnp.zeros(probs.shape, dtype=bool).at[rows, idx].set(keep_sorted)
            A = probs * mask
            return A / jnp.maximum(A.sum(-1, keepdims=True), 1e-12)
        N = X.shape[0]
        R = S + jnp.eye(N, dtype=X.dtype)
        R = R / R.sum(-1, keepdims=True)
        Z = jnp.zeros_like(X)
        Xf = X
        Xa = X
        for n in range(STEPS):
            A = _top_p_attention(Xa, W1, W2, W3)
            Xf = R @ Xf
            Xa = A @ Xa
            Z = Z + Xf @ U1[n].T + Xa @ U2[n].T
        h = X + Z
        mu = h.mean(-1, keepdims=True)
        var = jnp.mean((h - mu) ** 2, axis=-1, keepdims=True)
        return (h - mu) / jnp.sqrt(var + LN_EPS) * ln_g + ln_b
    x = _layernorm(x + _L0_gnn_ref(x, adj, L0_gnn_W, L0_gnn_a_l, L0_gnn_a_r), axis=-1)
    x = _layernorm(x + _L1_gnn_ref(x, adj, L1_gnn_W1, L1_gnn_W2, L1_gnn_W3, L1_gnn_U1, L1_gnn_U2, L1_gnn_ln_g, L1_gnn_ln_b), axis=-1)
    return x

_drawn_inputs = setup_inputs


def setup_inputs(seed=0):
    import zlib

    import numpy as np

    out = dict(_drawn_inputs(seed))
    spreads = {'L1_gnn_ln_g': (1.0, 0.2), 'L1_gnn_ln_b': (0.0, 0.1)}
    factors = {}
    for name, (base, spread) in spreads.items():
        noise = np.random.default_rng([zlib.crc32(name.encode()), seed]).standard_normal(out[name].shape)
        drawn = base * np.exp(spread * noise) if base else spread * noise
        out[name] = jnp.asarray(drawn.astype(out[name].dtype))
    for name, factor in factors.items():
        out[name] = (out[name] * factor).astype(out[name].dtype)
    return out
```

```python
from contextlib import ExitStack

import numpy as np

import concourse.bass as bass
from concourse import mybir

F32 = mybir.dt.float32
BF16 = mybir.dt.bfloat16
I32 = mybir.dt.int32
ALU = mybir.AluOpType
ACT = mybir.ActivationFunctionType
AX = mybir.AxisListType

P = 128
N = 4096
D = 128
HEADS = 4
DK = D // HEADS
DA = 64
STEPS = 2
T = N // P
TOP_P = 0.9
SLOPE = 0.2
EPS = 1e-5
MIN_SUM = 1e-12

CH = 4
NCH = T // CH
CW = CH * P
HC = DK + 1
GC = 2 * HC * HEADS
AC = HC * HEADS
PARTS = 3

SEG = 64
NSEG = N // SEG
NC = NSEG * 8
BIG = 1.5e38
SPAN = 5.5
FAST_STEPS = (6, 9)
FILL = 3
SLOW_STEPS = 28
LW = 1024
NL = N // LW
START = 1
XW = D + 1
SW = PARTS * D + 1


class Names:
    pass


class Steps:

    def __init__(self, eng, sem):
        self.eng, self.sem, self.base, self.n = eng, sem, START, 0

    def mark(self, ins):
        self.n += 1
        return ins.then_inc(self.sem, 1)

    def settle(self):
        self.eng.wait_ge(self.sem, self.base + self.n)

    def settle_apart(self, passed):
        wait_apart(self.eng, self.sem, self.base + self.n, passed)

    def done(self, ins):
        self.mark(ins)
        self.settle()

    def loop(self, i, per):
        self.before, self.per = self.base + self.n, per
        self.base, self.n = self.before + i * per, 0

    def leave(self, count):
        assert self.n == self.per, (self.n, self.per)
        self.base, self.n = self.before + count * self.per, 0


def wide(ap, count):
    return ap.unsqueeze(len(ap.shape)).broadcast_to([*ap.shape, count])


def wait_apart(eng, sem, value, passed):
    eng.wait_ge(sem, value)
    eng.sem_inc(passed, 1)


def sems(nc, used, phase, names):
    made = {name: nc.alloc_semaphore(f"{phase}_{name}") for name in names.split()}
    for sem in made.values():
        used.append(sem)
        nc.gpsimd.sem_inc(sem, START)
    return made


def phase(nc, write, *args):
    used = []
    write(nc, used, *args)
    nc.clear_and_free_semaphores(used)
    nc.all_engine_barrier()


def setup(nc, used, g, io):
    s = sems(nc, used, "setup", "loaded ident cleared pe evac steps stored")
    with ExitStack() as mem:
        def sb(name, shape, dt=F32):
            return mem.enter_context(nc.sbuf_tensor(name, shape, dt))

        W = sb("su_W", [P, D])
        W1 = sb("su_W1", [DA, D])
        W2 = sb("su_W2", [DA, DA])
        W3 = sb("su_W3", [DA, D])
        U = sb("su_U", [P, 2 * STEPS, D])
        WT = sb("su_WT", [P, D])
        al8 = sb("su_al8", [P, HEADS])
        arow = sb("su_arow", [P, 2, D])
        x_sb = sb("su_x", [P, T, D])
        xc = sb("su_xc", [P, CH, D])
        xT = sb("su_xT", [P, CW])
        WhT = sb("su_WhT", [P, CW])
        slrow = sb("su_slrow", [HEADS, N])
        prod = sb("su_prod", [P, T, D])
        tp = mem.enter_context(nc.psum_tensor("su_tp", [P, CW], F32))
        wh = mem.enter_context(nc.psum_tensor("su_wh", [P, CW], F32))
        whr = mem.enter_context(nc.psum_tensor("su_whr", [P, CH, D], F32))
        slp = mem.enter_context(nc.psum_tensor("su_slp", [P, CW], F32))
        NLOAD = 6 + 2 * STEPS + HEADS + 2 + 2
        with nc.Block() as block:
            @block.sync
            def _(sp):
                def load(dst, src):
                    sp.dma_start(dst, src).then_inc(s["loaded"], 16)

                load(W[:], io["W"])
                load(W1[:], io["W1"])
                load(W2[:], io["W2"])
                load(W3[:], io["W3"])
                for n in range(STEPS):
                    load(U[:, 2 * n, :], io["U1"][n])
                    load(U[:, 2 * n + 1, :], io["U2"][n])
                sp.wait_ge(s["cleared"], START + 1)
                for h in range(HEADS):
                    load(al8[h * DK:(h + 1) * DK, h:h + 1], io["a_l"][h].rearrange("(d o) -> d o", o=1))
                for k, a in enumerate((io["a_l"], io["a_r"])):
                    load(arow[:, k, :], a.rearrange("h d -> (h d)").rearrange("(o k) -> o k", o=1).to_broadcast([P, D]))
                for k, v in enumerate((io["ln_g"], io["ln_b"])):
                    load(g.gb[:, k, :], v.rearrange("(o k) -> o k", o=1).to_broadcast([P, D]))
                load(x_sb[:], io["x"].rearrange("(t p) d -> p t d", p=P))
                sp.dma_start(g.diag[:], bass.AP(io["adj"].tensor, io["adj"].offset, [[N + 1, P], [(N + 1) * P, T], [1, 1]]),
                             allow_slow_non_contiguous=True).then_inc(s["loaded"], 16)
                sp.wait_ge(s["evac"], START + 4 * NCH + 1)
                sp.dma_start(g.sl_dram, slrow[:]).then_inc(s["stored"], 16)
                sp.wait_ge(s["stored"], START + 16)

            @block.gpsimd
            def _(pool):
                nc.gpsimd.memset(g.ident[:], 1.0).then_inc(s["ident"], 1)
                nc.gpsimd.memset(g.ones[:], 1.0).then_inc(s["ident"], 1)
                nc.gpsimd.memset(g.tri[:], 1.0).then_inc(s["ident"], 1)
                pool.wait_ge(s["ident"], START + 3)
                nc.gpsimd.affine_select(out=g.ident[:], in_=g.ident[:], compare_op=ALU.is_equal, fill=0.0,
                                        base=0, pattern=[[1, P]], channel_multiplier=-1).then_inc(s["ident"], 1)
                nc.gpsimd.affine_select(out=g.tri[:], in_=g.tri[:], compare_op=ALU.is_gt, fill=0.0,
                                        base=0, pattern=[[1, P]], channel_multiplier=-1).then_inc(s["ident"], 1)
                nc.gpsimd.iota(g.iota[:], pattern=[[1, P]], base=0, channel_multiplier=0,
                               allow_small_or_imprecise_dtypes=True).then_inc(s["ident"], 1)

            @block.tensor
            def _(pe):
                pe.wait_ge(s["loaded"], START + 16 * NLOAD)
                pe.wait_ge(s["ident"], START + 6)
                nc.tensor.transpose(tp[:, 0:D], W[:], g.ident[:])
                nc.tensor.transpose(tp[:, D:D + DA], W1[:], g.ident[0:DA, 0:DA])
                nc.tensor.transpose(tp[:, 192:192 + DA], W3[:], g.ident[0:DA, 0:DA])
                nc.tensor.transpose(tp[0:DA, 256:256 + DA], W2[:], g.ident[0:DA, 0:DA])
                for k in range(2 * STEPS):
                    last = nc.tensor.transpose(whr[:, k, :], U[:, k, :], g.ident[:])
                last.then_inc(s["pe"], 1)
                with pe.Fori(0, NCH) as c:
                    pe.wait_ge(s["evac"], START + 4 * c + 2)
                    for j in range(CH):
                        last = nc.tensor.transpose(tp[:, j * P:(j + 1) * P], xc[:, j, :], g.ident[:])
                    last.then_inc(s["pe"], 1)
                    pe.wait_ge(s["evac"], START + 4 * c + 3)
                    nc.tensor.matmul(wh[:], WT[:], xT[:], start=True, stop=True)
                    for j in range(CH):
                        last = nc.tensor.matmul(whr[:, j, :], xT[:, j * P:(j + 1) * P], WT[:], start=True, stop=True)
                    last.then_inc(s["pe"], 1)
                    pe.wait_ge(s["evac"], START + 4 * c + 4)
                    nc.tensor.matmul(slp[0:HEADS, :], al8[:], WhT[:], start=True, stop=True).then_inc(s["pe"], 1)

            @block.vector
            def _(dve):
                nc.vector.memset(al8[:], 0.0).then_inc(s["cleared"], 1)
                st = Steps(dve, s["steps"])
                dve.wait_ge(s["pe"], START + 1)
                st.mark(nc.vector.tensor_copy(WT[:], tp[:, 0:D]))
                st.mark(nc.vector.tensor_copy(g.W1T[:], tp[:, D:D + DA]))
                st.mark(nc.vector.tensor_copy(g.W3T[:], tp[:, 192:192 + DA]))
                st.mark(nc.vector.tensor_copy(g.W2T[:], tp[0:DA, 256:256 + DA]))
                nc.vector.tensor_copy(g.UT[:], whr[:]).then_inc(s["evac"], 1)
                st.settle()
                dve.wait_ge(s["loaded"], START + 16 * NLOAD)
                with dve.Fori(0, NCH) as c:
                    nc.vector.tensor_copy(xc[:], x_sb[:, bass.ds(CH * c, CH), :]).then_inc(s["evac"], 1)
                    dve.wait_ge(s["pe"], START + 3 * c + 2)
                    nc.vector.tensor_copy(xT[:], tp[:]).then_inc(s["evac"], 1)
                    dve.wait_ge(s["pe"], START + 3 * c + 3)
                    nc.vector.tensor_copy(WhT[:], wh[:]).then_inc(s["evac"], 1)
                    st.loop(c, 1)
                    st.mark(nc.vector.tensor_copy(
                        g.WhA[:, bass.ds(CH * c, CH), :].rearrange("p t (h e) -> p (t h) e", e=HC)[:, :, 0:DK],
                        whr[:].rearrange("p t (h d) -> p (t h) d", d=DK)))
                    dve.wait_ge(s["pe"], START + 3 * c + 4)
                    st.settle()
                    nc.vector.tensor_copy(slrow[:, bass.ds(CW * c, CW)], slp[0:HEADS, :]).then_inc(s["evac"], 1)
                st.leave(NCH)
                st.done(nc.vector.memset(g.WhA[:].rearrange("p t (h e) -> p (t h) e", e=HC)[:, :, DK:HC], 1.0))
                Wh = g.WhA[:].rearrange("p t (h e) -> p (t h) e", e=HC)[:, :, 0:DK]
                pr = prod[:].rearrange("p t (h d) -> p (t h) d", d=DK)
                for k, score in enumerate((g.sl, g.sr)):
                    for t in range(HEADS):
                        st.mark(nc.vector.tensor_tensor(
                            prod[:, :, t * DK:(t + 1) * DK],
                            g.WhA[:, :, t * HC:t * HC + DK],
                            arow[:, k:k + 1, t * DK:(t + 1) * DK].broadcast_to([P, T, DK]), ALU.mult))
                    st.settle()
                    st.done(nc.vector.tensor_reduce(score[:].rearrange("p t h -> p (t h)"), pr, AX.X, ALU.add))


def tables(nc, used, g, io, G, slb):
    s = sems(nc, used, "tab", "rows pe steps exps")
    with ExitStack() as mem:
        def sb(name, shape, dt=F32):
            return mem.enter_context(nc.sbuf_tensor(name, shape, dt))

        top = sb("tb_top", [P, HEADS])
        m4 = sb("tb_m4", [HEADS, 1])
        d4 = sb("tb_d4", [HEADS, HEADS])
        mb = sb("tb_mb", [P, 1, HEADS])
        srm = sb("tb_srm", [P, T, HEADS])
        slm = sb("tb_slm", [P, T, HEADS])
        top_n = sb("tb_topn", [P, T, HEADS])
        a2 = sb("tb_a2", [P, T, HEADS])
        xs = sb("tb_self", [P, T, HEADS])
        F1 = sb("tb_F1", [P, T, HEADS])
        F2 = sb("tb_F2", [P, T, HEADS])
        off = sb("tb_off", [P, T])
        G32 = sb("tb_G32", [P, T, GC])
        pt = mem.enter_context(nc.psum_tensor("tb_pt", [P, CW], F32))
        pb = mem.enter_context(nc.psum_tensor("tb_pb", [P, CW], F32))
        with nc.Block() as block:
            @block.sync
            def _(sp):
                for h in range(HEADS):
                    sp.dma_start(slb[:, h, :], g.sl_dram[h:h + 1, :].to_broadcast([P, N])).then_inc(s["rows"], 16)
                sp.wait_ge(s["rows"], START + 16 * HEADS)

            @block.tensor
            def _(pe):
                pe.wait_ge(s["steps"], START + 1)
                nc.tensor.transpose(pt[0:HEADS, 0:P], top[:], g.ident[:]).then_inc(s["pe"], 1)
                pe.wait_ge(s["steps"], START + 3)
                nc.tensor.matmul(pb[:, 0:HEADS], g.ones[0:HEADS, :], d4[:], start=True, stop=True).then_inc(s["pe"], 1)

            @block.vector
            def _(dve):
                st = Steps(dve, s["steps"])
                st.done(nc.vector.tensor_reduce(top[:], g.sr[:].rearrange("p t h -> p h t"), AX.X, ALU.max))
                dve.wait_ge(s["pe"], START + 1)
                st.done(nc.vector.tensor_reduce(m4[:], pt[0:HEADS, 0:P], AX.X, ALU.max))
                st.done(nc.vector.tensor_scalar(d4[:], g.ident[0:HEADS, 0:HEADS], m4[:], None, ALU.mult))
                dve.wait_ge(s["pe"], START + 2)
                st.done(nc.vector.tensor_copy(mb[:, 0, :], pb[:, 0:HEADS]))
                over_t = mb[:].broadcast_to([P, T, HEADS])
                st.mark(nc.vector.tensor_tensor(srm[:], g.sr[:], over_t, ALU.subtract))
                st.mark(nc.vector.tensor_tensor(slm[:], g.sl[:], over_t, ALU.add))
                st.mark(nc.vector.tensor_tensor(xs[:], g.sl[:], g.sr[:], ALU.add))
                st.mark(nc.vector.tensor_scalar(g.nsr[:], g.sr[:], -1.0, None, ALU.mult))
                st.mark(nc.vector.tensor_scalar(off[:], g.diag[:, :, 0], 1.0, None, ALU.min))
                st.settle()
                st.mark(nc.vector.scalar_tensor_tensor(out=top_n[:], in0=slm[:], scalar=SLOPE, in1=slm[:],
                                                       op0=ALU.mult, op1=ALU.max))
                st.mark(nc.vector.scalar_tensor_tensor(out=xs[:], in0=xs[:], scalar=SLOPE, in1=xs[:],
                                                       op0=ALU.mult, op1=ALU.max))
                st.mark(nc.vector.tensor_scalar(off[:], off[:], -1.0, 1.0, ALU.mult, ALU.add))
                st.settle()
                st.mark(nc.vector.scalar_tensor_tensor(out=a2[:], in0=slm[:], scalar=SLOPE, in1=top_n[:],
                                                       op0=ALU.mult, op1=ALU.subtract))
                st.mark(nc.vector.tensor_tensor(xs[:], xs[:], top_n[:], ALU.subtract))
                st.done(nc.vector.tensor_tensor(slm[:], slm[:], top_n[:], ALU.subtract))
                dve.wait_ge(s["exps"], START + 5)
                st.mark(nc.vector.tensor_tensor(g.selfp[:], g.selfp[:], wide(off[:], HEADS), ALU.mult))
                heads = g.WhA[:].rearrange("p t (h e) -> p (t h) e", e=HC)
                table = G32[:].rearrange("p t (h k e) -> p (t h) k e", k=2, e=HC)
                for k, F in enumerate((F1, F2)):
                    st.mark(nc.vector.tensor_tensor(table[:, :, k, :], heads,
                                                    wide(F[:].rearrange("p t h -> p (t h)"), HC), ALU.mult))
                st.settle()
                for k in range(PARTS):
                    st.done(nc.vector.tensor_copy(G[:, :, k, :], G32[:]))
                    if k < PARTS - 1:
                        st.done(nc.vector.tensor_tensor(G32[:], G32[:], G[:, :, k, :], ALU.subtract))

            @block.scalar
            def _(act):
                act.wait_ge(s["steps"], START + 15)
                for out, x, scale in ((F1, srm, 1.0), (F2, srm, SLOPE), (g.E1, slm, 1.0), (g.E2, a2, 1.0),
                                      (g.selfp, xs, 1.0)):
                    nc.scalar.activation(out[:], x[:], ACT.Exp, scale=scale).then_inc(s["exps"], 1)


def gat(nc, used, g, io, G, slb):
    UM = 4
    UB = T // UM
    s = sems(nc, used, "gat", "zeroed acc copied pooled psteps")
    slots = [sems(nc, used, f"gat_slot{r}", "rows_in rows_read stored adj_used") for r in range(2)]
    banks = [sems(nc, used, f"gat_bank{v}", "turned evac masks sums") for v in range(UM)]
    with ExitStack() as mem:
        def sb(name, shape, dt=F32):
            return mem.enter_context(nc.sbuf_tensor(name, shape, dt))

        rows = [sb(f"ga_rows{r}", [P, CH, UM * P]) for r in range(2)]
        aT = [sb(f"ga_aT{r}", [P, CH, UM, P], BF16) for r in range(2)]
        B = [sb(f"ga_B{v}", [P, HEADS, CH, P], BF16) for v in range(UM)]
        zero = sb("ga_zero", [P, P], BF16)
        accs = sb("ga_accs", [P, CH, GC + AC])
        w1 = sb("ga_w1", [P, HEADS, HC])
        w2 = sb("ga_w2", [P, HEADS, HC])
        w3 = sb("ga_w3", [P, HEADS, HC])
        acc = mem.enter_context(nc.psum_tensor("ga_acc", [P, CH, CW], F32))
        tp = [mem.enter_context(nc.psum_tensor(f"ga_tp{v}", [P, CH, P], F32)) for v in range(UM)]
        adj = io["adj"].rearrange("(t p) m -> p t m", p=P)
        adjT = g.adjT.rearrange("t p m -> p t m")

        with nc.Block() as block:
            @block.sync
            def _(sp):
                with sp.Fori(0, NCH) as b:
                    with sp.Fori(0, UB // 2) as q:
                        for r in range(2):
                            use = (UB // 2) * b + q
                            sp.wait_ge(slots[r]["rows_read"], START + use)
                            sp.dma_start(rows[r][:], adj[:, bass.ds(CH * b, CH), bass.ds((2 * q + r) * (UM * P), UM * P)]
                                         ).then_inc(slots[r]["rows_in"], 16)

            @block.gpsimd
            def _(pool):
                st = Steps(pool, s["psteps"])
                nc.gpsimd.memset(zero[:], 0.0).then_inc(s["zeroed"], 1)

                def of_tile(x, t):
                    return x[:, bass.ds(t, 1), :].rearrange("p o c -> p (o c)")

                with pool.Fori(0, NCH) as b:
                    pool.wait_ge(s["copied"], START + b + 1)
                    st.loop(b, 6 * CH)
                    for j in range(CH):
                        t = CH * b + j
                        half = accs[:, j, 0:GC].rearrange("p (h k e) -> p h k e", k=2, e=HC)
                        both = accs[:, j, GC:].rearrange("p (h e) -> p h e", e=HC)
                        own = of_tile(g.WhA, t).rearrange("p (h e) -> p h e", e=HC)
                        st.mark(nc.gpsimd.tensor_tensor(w1[:], both, half[:, :, 1, :], ALU.subtract))
                        st.mark(nc.gpsimd.tensor_tensor(w2[:], half[:, :, 0, :], wide(of_tile(g.E1, t), HC), ALU.mult))
                        st.mark(nc.gpsimd.tensor_tensor(w3[:], own, wide(of_tile(g.selfp, t), HC), ALU.mult))
                        st.settle()
                        st.mark(nc.gpsimd.tensor_tensor(w1[:], w1[:], wide(of_tile(g.E2, t), HC), ALU.mult))
                        st.done(nc.gpsimd.tensor_tensor(w2[:], w2[:], w3[:], ALU.add))
                        st.done(nc.gpsimd.tensor_tensor(of_tile(g.gsum, t).rearrange("p (h e) -> p h e", e=HC),
                                                        w1[:], w2[:], ALU.add))
                    st.leave(NCH)

            @block.tensor
            def _(pe):
                pe.wait_ge(s["zeroed"], START + 1)
                any_row = G[:].rearrange("p t k c -> p (t k c)")[:, 0:GC + AC]

                def turn(b, q, u):
                    unit = UB * b + 2 * q + u
                    pe.wait_ge(slots[u % 2]["rows_in"], START + 16 * ((UB // 2) * b + q + u // 2) + 16)
                    for v in range(UM):
                        pe.wait_ge(banks[v]["evac"], START + unit)
                        for j in range(CH):
                            last = nc.tensor.transpose(tp[v][:, j, :], rows[u % 2][:, j, v * P:(v + 1) * P], g.ident[:])
                        last.then_inc(banks[v]["turned"], 1)

                def product(b, q, r, turned):
                    unit = UB * b + 2 * q + r
                    turned = list(turned)
                    for v in range(UM):
                        m = bass.ds((2 * q + r) * UM + v, 1)
                        pe.wait_ge(banks[v]["evac"], START + unit + 1)
                        for j in range(CH):
                            for k in range(PARTS):
                                table = G[:, m, k, :].rearrange("p o (h k e) -> p (o h) k e", k=2, e=HC)
                                last = nc.tensor.matmul(
                                    acc[:, j, GC:GC + AC].rearrange("p (h e) -> p h e", e=HC),
                                    aT[r][:, j, v, :], table[:, :, 1, :], start=False, stop=False,
                                    skip_group_check=True)
                                if turned:
                                    last.then_inc(slots[turned.pop(0)]["rows_read"], 1)
                        pe.wait_ge(banks[v]["masks"], START + unit + 1)
                        for j in range(CH):
                            for h in range(HEADS):
                                for k in range(PARTS):
                                    cols = slice(h * 2 * HC, (h + 1) * 2 * HC)
                                    last = nc.tensor.matmul(
                                        acc[:, j, cols], B[v][:, h, j, :],
                                        G[:, m, k, cols].rearrange("p o c -> p (o c)"),
                                        start=False, stop=False, skip_group_check=True)
                                    if v == UM - 1 and j == 0 and h == 0 and k == 0:
                                        last.then_inc(slots[r]["adj_used"], 1)
                        last.then_inc(banks[v]["sums"], 1)

                with pe.Fori(0, NCH) as b:
                    pe.wait_ge(s["copied"], START + b)
                    for j in range(CH):
                        nc.tensor.matmul(acc[:, j, 0:GC + AC], zero[:], any_row, start=True, stop=False,
                                         skip_group_check=True)
                    turn(b, 0, 0)
                    turn(b, 0, 1)
                    product(b, 0, 0, (0, 1))
                    with pe.Fori(0, UB // 2 - 1) as q:
                        turn(b, q, 2)
                        product(b, q, 1, (0,))
                        turn(b, q, 3)
                        product(b, q + 1, 0, (1,))
                    product(b, UB // 2 - 1, 1, ())
                    for j in range(CH):
                        last = nc.tensor.matmul(acc[:, j, 0:GC + AC], zero[:], any_row, start=False, stop=True,
                                                skip_group_check=True)
                    last.then_inc(s["acc"], 1)

            @block.vector
            def _(dve):
                with dve.Fori(0, NCH) as b:
                    with dve.Fori(0, UB // 2) as q:
                        for r in range(2):
                            unit = UB * b + 2 * q + r
                            for v in range(UM):
                                dve.wait_ge(banks[v]["evac"], START + unit + 1)
                                dve.wait_ge(banks[v]["sums"], START + unit)
                                m = (2 * q + r) * UM + v
                                for h in range(HEADS):
                                    last = nc.vector.scalar_tensor_tensor(
                                        out=B[v][:, h], in0=slb[:, h, bass.ds(CW * b, CW)].rearrange("p (j n) -> p j n", n=P),
                                        scalar=g.nsr[:, bass.ds(m, 1), h], in1=aT[r][:, :, v, :],
                                        op0=ALU.is_ge, op1=ALU.mult)
                                last.then_inc(banks[v]["masks"], 1)

            @block.scalar
            def _(act):
                with act.Fori(0, NCH) as b:
                    with act.Fori(0, UB // 2) as q:
                        for r in range(2):
                            unit = UB * b + 2 * q + r
                            use = (UB // 2) * b + q
                            act.wait_ge(slots[r]["stored"], START + 16 * use)
                            act.wait_ge(slots[r]["adj_used"], START + use)
                            for v in range(UM):
                                act.wait_ge(banks[v]["turned"], START + unit + 1)
                                nc.scalar.activation(aT[r][:, :, v, :], tp[v][:], ACT.Copy).then_inc(banks[v]["evac"], 1)
                            for v in range(UM):
                                act.wait_ge(banks[v]["evac"], START + unit + 1)
                            act.dma_start(adjT[:, bass.ds(CH * b, CH), bass.ds((2 * q + r) * (UM * P), UM * P)],
                                          aT[r][:].rearrange("p j v n -> p j (v n)")).then_inc(slots[r]["stored"], 16)
                    act.wait_ge(s["acc"], START + b + 1)
                    act.wait_ge(s["psteps"], START + 6 * CH * b)
                    nc.scalar.activation(accs[:], acc[:, :, 0:GC + AC], ACT.Copy).then_inc(s["copied"], 1)
                for r in range(2):
                    act.wait_ge(slots[r]["stored"], START + 16 * (NCH * UB // 2))


def norm_before(st, nc, x, c, sq, stat):
    st.done(nc.vector.tensor_reduce(stat[:, 0, :], x, AX.X, ALU.add))
    st.done(nc.vector.tensor_scalar(stat[:, 0, :], stat[:, 0, :], 1.0 / D, None, ALU.mult))
    st.done(nc.vector.tensor_tensor(c, x, wide(stat[:, 0, :], D), ALU.subtract))
    st.done(nc.vector.tensor_tensor(sq, c, c, ALU.mult))
    st.done(nc.vector.tensor_reduce(stat[:, 0, :], sq, AX.X, ALU.add))
    st.done(nc.vector.tensor_scalar(stat[:, 0, :], stat[:, 0, :], 1.0 / D, EPS, ALU.mult, ALU.add))


def norm_after(st, nc, c, out, stat):
    st.done(nc.vector.reciprocal(stat[:, 0, :], stat[:, 1, :]))
    st.done(nc.vector.tensor_tensor(out, c, wide(stat[:, 0, :], D), ALU.mult))


def first_norm(nc, used, g, io):
    s = sems(nc, used, "n1", "loaded steps low exps stds stored")
    with ExitStack() as mem:
        x_sb = mem.enter_context(nc.sbuf_tensor("n1_x", [P, T, D], F32))
        w = mem.enter_context(nc.sbuf_tensor("n1_w", [P, T, D], F32))
        w2 = mem.enter_context(nc.sbuf_tensor("n1_w2", [P, T, D], F32))
        stat = mem.enter_context(nc.sbuf_tensor("n1_stat", [P, 2, T], F32))
        rden = mem.enter_context(nc.sbuf_tensor("n1_rden", [P, T * HEADS], F32))
        with nc.Block() as block:
            @block.sync
            def _(sp):
                sp.dma_start(x_sb[:], io["x"].rearrange("(t p) d -> p t d", p=P)).then_inc(s["loaded"], 16)
                sp.wait_ge(s["steps"], START + 12)
                sp.dma_start(g.x1_dram.rearrange("(t p) d -> p t d", p=P), w2[:]).then_inc(s["stored"], 16)
                sp.wait_ge(s["stored"], START + 16)

            @block.vector
            def _(dve):
                st = Steps(dve, s["steps"])
                sums = g.gsum[:].rearrange("p t (h e) -> p (t h) e", e=HC)
                st.done(nc.vector.reciprocal(rden[:], sums[:, :, DK]))
                st.done(nc.vector.tensor_tensor(w[:].rearrange("p t (h d) -> p (t h) d", d=DK), sums[:, :, 0:DK],
                                                wide(rden[:], DK), ALU.mult))
                nc.vector.tensor_scalar(w2[:], w[:], 0.0, None, ALU.min).then_inc(s["low"], 1)
                dve.wait_ge(s["exps"], START + 1)
                st.done(nc.vector.scalar_tensor_tensor(out=w[:], in0=w[:], scalar=0.0, in1=w2[:],
                                                       op0=ALU.max, op1=ALU.add))
                dve.wait_ge(s["loaded"], START + 16)
                st.done(nc.vector.scalar_tensor_tensor(out=w[:], in0=w[:], scalar=-1.0, in1=x_sb[:],
                                                       op0=ALU.add, op1=ALU.add))
                norm_before(st, nc, w[:], w[:], w2[:], stat)
                dve.wait_ge(s["stds"], START + 1)
                norm_after(st, nc, w[:], w2[:], stat)
                assert st.n == 12

            @block.scalar
            def _(act):
                act.wait_ge(s["low"], START + 1)
                nc.scalar.activation(w2[:], w2[:], ACT.Exp).then_inc(s["exps"], 1)
                act.wait_ge(s["steps"], START + 10)
                nc.scalar.activation(stat[:, 1, :], stat[:, 0, :], ACT.Sqrt).then_inc(s["stds"], 1)


def place_x1(nc, used, g):
    s = sems(nc, used, "px", "ones loaded")
    with nc.Block() as block:
        @block.sync
        def _(sp):
            x1 = g.x1_dram.rearrange("(t p) d -> p t d", p=P)
            for dst in (g.xa[0][:, :, 0:D], g.xf[:]):
                sp.dma_start(dst, x1).then_inc(s["loaded"], 16)
            sp.wait_ge(s["loaded"], START + 32)

        @block.vector
        def _(dve):
            for ones in (g.xa[0][:, :, D:XW], g.xa[1][:, :, D:XW], g.xs[:, :, PARTS * D:SW]):
                nc.vector.memset(ones, 1.0).then_inc(s["ones"], 1)
            dve.wait_ge(s["ones"], START + 3)


def project(nc, used, g, step, h=None):
    s = sems(nc, used, f"pr{step}", "pe cut steps loaded stored divided parts passed")
    with ExitStack() as mem:
        def sb(name, shape, dt=F32):
            return mem.enter_context(nc.sbuf_tensor(f"pr{step}_{name}", shape, dt))

        def ps(name, shape):
            return mem.enter_context(nc.psum_tensor(f"pr{step}_{name}", shape, F32))

        xc = sb("xc", [P, 2, CH, D])
        xT = sb("xT", [P, 2, CW])
        w1 = sb("w1", [DA, CW])
        rinv = sb("rinv", [P, T])
        work = sb("work", [P, T, D])
        tp = ps("tp", [P, 2, CW])
        z = ps("z", [P, CH, D])
        qk = ps("qk", [DA, 3, CW])
        xa = g.xa[step % 2]
        more = step < STEPS
        both = step > 0
        NP = 1 + both + 2 * more
        with nc.Block() as block:
            @block.sync
            def _(sp):
                if both:
                    h_dram = (g.x1_dram if step == 1 else g.h_dram).rearrange("(t p) d -> p t d", p=P)
                    sp.dma_start(h[:], h_dram).then_inc(s["loaded"], 16)
                    if more:
                        sp.wait_ge(s["cut"], START + (3 + more) * NCH)
                        sp.dma_start(g.h_dram.rearrange("(t p) d -> p t d", p=P), h[:]).then_inc(s["stored"], 16)
                        sp.wait_ge(s["stored"], START + 16)

            @block.tensor
            def _(pe):
                with pe.Fori(0, NCH) as c:
                    pe.wait_ge(s["cut"], START + (3 + more) * c + 1)
                    for j in range(CH):
                        last = nc.tensor.transpose(tp[:, 0, j * P:(j + 1) * P], xc[:, 0, j, :], g.ident[:])
                        if both:
                            last = nc.tensor.transpose(tp[:, 1, j * P:(j + 1) * P], xc[:, 1, j, :], g.ident[:])
                    last.then_inc(s["pe"], 1)
                    pe.wait_ge(s["cut"], START + (3 + more) * c + 2)
                    if both:
                        for j in range(CH):
                            cols = slice(j * P, (j + 1) * P)
                            nc.tensor.matmul(z[:, j, :], xT[:, 1, cols], g.UT[:, 2 * step - 2, :], start=True, stop=False)
                            last = nc.tensor.matmul(z[:, j, :], xT[:, 0, cols], g.UT[:, 2 * step - 1, :],
                                                    start=False, stop=True)
                        last.then_inc(s["pe"], 1)
                    if more:
                        nc.tensor.matmul(qk[:, 0, :], g.W1T[:], xT[:, 0, :], start=True, stop=True)
                        nc.tensor.matmul(qk[:, 1, :], g.W3T[:], xT[:, 0, :], start=True, stop=True).then_inc(s["pe"], 1)
                        wait_apart(pe, s["cut"], START + (3 + more) * c + 3, s["passed"])
                        nc.tensor.matmul(qk[:, 2, :], g.W2T[:], w1[:], start=True, stop=True).then_inc(s["pe"], 1)

            @block.gpsimd
            def _(pool):
                if more:
                    st = Steps(pool, s["parts"])
                    if both:
                        pool.wait_ge(s["divided"], START + 1)
                    for k in range(PARTS):
                        part = g.xs[:, :, k * D:(k + 1) * D]
                        st.done(nc.gpsimd.tensor_copy(part, g.xf[:] if k == 0 else work[:]))
                        if k < PARTS - 1:
                            st.done(nc.gpsimd.tensor_tensor(work[:], g.xf[:] if k == 0 else work[:], part,
                                                            ALU.subtract))

            @block.vector
            def _(dve):
                st = Steps(dve, s["steps"])
                if both:
                    st.done(nc.vector.reciprocal(rinv[:], g.rsum[:]))
                    nc.vector.tensor_tensor(g.xf[:], g.xf[:], wide(rinv[:], D), ALU.mult).then_inc(s["divided"], 1)
                    dve.wait_ge(s["divided"], START + 1)
                if both:
                    dve.wait_ge(s["loaded"], START + 16)
                with dve.Fori(0, NCH) as c:
                    tiles = bass.ds(CH * c, CH)
                    st.loop(c, both + more + (both and more))
                    if both:
                        st.mark(nc.vector.tensor_copy(xc[:, 1], g.xf[:, tiles, :]))
                        st.settle()
                    nc.vector.tensor_copy(xc[:, 0], xa[:, tiles, 0:D]).then_inc(s["cut"], 1)
                    dve.wait_ge(s["pe"], START + NP * c + 1)
                    w = slice(0, 1 + both)
                    nc.vector.tensor_copy(xT[:, w, :], tp[:, w, :]).then_inc(s["cut"], 1)
                    if more:
                        dve.wait_ge(s["pe"], START + NP * c + 2 + both)
                        nc.vector.tensor_copy(w1[:], qk[:, 0, :]).then_inc(s["cut"], 1)
                        st.mark(nc.vector.tensor_copy(g.qkT[0:DA, bass.ds(CW * c, CW)], qk[:, 1, :]))
                        dve.wait_ge(s["pe"], START + NP * c + 3 + both)
                        st.settle()
                        last = nc.vector.tensor_copy(g.qkT[DA:P, bass.ds(CW * c, CW)], qk[:, 2, :])
                    if both:
                        dve.wait_ge(s["pe"], START + NP * c + 2)
                        if more:
                            st.done(last)
                        last = nc.vector.tensor_tensor(h[:, tiles, :], h[:, tiles, :], z[:], ALU.add)
                    last.then_inc(s["cut"], 1)
                st.leave(NCH)


def attend(nc, used, g, step, buf):
    s = sems(nc, used, f"at{step}", "padded steps rsums_out values_out psteps passed")
    slots = [sems(nc, used, f"at{step}_slot{j}", "q cand ecand terms top8 e8 mask out rin rsums rpool") for j in range(2)]
    lbank = [sems(nc, used, f"at{step}_lbank{x}", "made read") for x in range(2)]
    tbank = [sems(nc, used, f"at{step}_tbank{x}", "made") for x in range(2)]
    ring = [sems(nc, used, f"at{step}_ring{y}", "filled used") for y in range(4)]
    xa, xa_new = g.xa[step % 2], g.xa[(step + 1) % 2]
    b = buf
    halvings = FAST_STEPS[step]
    NG = T // CH
    PAIRS = T // 2

    with nc.Block() as block:
        @block.sync
        def _(sp):
            with sp.Fori(0, PAIRS) as i:
                for j in range(2):
                    sp.wait_ge(slots[j]["rsums"], START + i)
                    sp.dma_start(b.rt[j][:].rearrange("p m n -> p (m n)"),
                                 g.adjT[bass.ds(2 * i + j, 1), :, :].rearrange("o p m -> (o p) m")
                                 ).then_inc(slots[j]["rin"], 16)

        @block.gpsimd
        def _(pool):
            st = Steps(pool, s["psteps"])
            with pool.Fori(0, PAIRS) as i:
                st.loop(i, 6)
                for j in range(2):
                    t = bass.ds(2 * i + j, 1)
                    rs = b.rsums[j]
                    xf_t = g.xf[:, t, :].rearrange("p o d -> p (o d)")
                    pool.wait_ge(s["rsums_out"], START + 2 * i + j + 1)
                    st.mark(nc.gpsimd.tensor_tensor(rs[:, D:2 * D], rs[:, D:2 * D], rs[:, 2 * D:3 * D], ALU.add))
                    st.mark(nc.gpsimd.tensor_tensor(xf_t, xf_t, rs[:, 0:D], ALU.add))
                    st.settle()
                    st.mark(nc.gpsimd.tensor_tensor(g.rsum[:, t], rs[:, 3 * D:SW], g.ones[:, 0:1], ALU.add))
                    nc.gpsimd.tensor_tensor(xf_t, xf_t, rs[:, D:2 * D], ALU.add).then_inc(slots[j]["rpool"], 1)
                st.leave(PAIRS)

        @block.tensor
        def _(pe):
            def logits(i, c):
                j, t = c % 2, 2 * i + c
                pe.wait_ge(slots[j]["q"], START + i + c // 2 + 1)
                for n in range(NL):
                    x = n % 2
                    pe.wait_ge(lbank[x]["read"], START + 2 * t + n // 2)
                    for k in range(LW // CW):
                        cols = slice(n * LW + k * CW, n * LW + (k + 1) * CW)
                        last = nc.tensor.matmul(b.lp[x][:, k, :], b.qt[j][:], g.qkT[:, cols], start=True, stop=True)
                    last.then_inc(lbank[x]["made"], 1)

            def neighbours(i, c):
                j, t = c % 2, 2 * i + c
                pe.wait_ge(slots[j]["rin"], START + 16 * (i + c // 2) + 16)
                pe.wait_ge(s["rsums_out"], START + t)
                for m in range(T):
                    last = nc.tensor.matmul(b.racc[:, 0:SW], b.rt[j][:, m, :], g.xs[:, m, :], start=(m == 0),
                                            stop=(m == T - 1))
                last.then_inc(slots[j]["rsums"], 1)

            def turn(i, c, k):
                pe.wait_ge(ring[(k - 2) % 4]["filled"], START + 2 * (2 * i + c) + (k - 2) // 4 + 1)
                for n in range(CH):
                    m = CH * k + n
                    last = nc.tensor.transpose(b.tp[k % 2][:, n, :], b.e[c % 2][:, m * P:(m + 1) * P], g.ident[:])
                last.then_inc(tbank[k % 2]["made"], 1)

            def apply(i, c, k):
                y = k % 4
                pe.wait_ge(ring[y]["filled"], START + 2 * (2 * i + c) + k // 4 + 1)
                for n in range(CH):
                    m = CH * k + n
                    last = nc.tensor.matmul(b.o[:, 0:XW], b.aT[y][:, n, :], xa[:, m, :], start=(m == 0),
                                            stop=(m == T - 1))
                last.then_inc(ring[y]["used"], 1)

            def values(i, c):
                pe.wait_ge(slots[c % 2]["mask"], START + i + c // 2 + 1)
                pe.wait_ge(s["values_out"], START + 2 * i + c)
                for k in range(NG + 1):
                    if k < NG:
                        turn(i, c, k)
                    if k > 0:
                        apply(i, c, k - 1)

            pe.wait_ge(s["padded"], START + 2)
            for c in range(2):
                logits(0, c)
            for c in range(2):
                neighbours(0, c)
            with pe.Fori(0, PAIRS - 1) as i:
                for c in range(2):
                    logits(i, c + 2)
                    values(i, c)
                    neighbours(i, c + 2)
            for c in range(2):
                values(PAIRS - 1, c)

        @block.scalar
        def _(act):
            def query(i, c):
                if c >= 2:
                    act.wait_ge(lbank[1]["made"], START + 2 * (2 * i + c - 1))
                nc.scalar.activation(b.qt[c % 2][0:DA], g.qkT[DA:P, bass.ds((2 * i + c) * P, P)], ACT.Copy
                                     ).then_inc(slots[c % 2]["q"], 1)

            def logits(i, c):
                act.wait_ge(slots[c % 2]["mask"], START + i + c // 2)
                for n in range(NL):
                    x = n % 2
                    act.wait_ge(lbank[x]["made"], START + 2 * (2 * i + c) + n // 2 + 1)
                    nc.scalar.activation(b.l[c % 2][:, n * LW:(n + 1) * LW], b.lp[x][:].rearrange("p k n -> p (k n)"),
                                         ACT.Copy).then_inc(lbank[x]["read"], 1)

            def sums(i, c):
                j = c % 2
                act.wait_ge(slots[j]["rsums"], START + i + c // 2 + 1)
                act.wait_ge(slots[j]["rpool"], START + i + c // 2)
                nc.scalar.activation(b.rsums[j][:], b.racc[:, 0:SW], ACT.Copy).then_inc(s["rsums_out"], 1)

            def terms(i, c):
                j = c % 2
                act.wait_ge(slots[j]["cand"], START + i + c // 2 + 1)
                nc.scalar.activation(b.ec[j][:], b.lc[j][:], ACT.Exp, bias=b.negmax[j][:]).then_inc(slots[j]["ecand"], 1)
                if c >= 2:
                    act.wait_ge(ring[3]["used"], START + 2 * (2 * i + c - 1))
                nc.scalar.activation(b.e[j][:], b.l[j][:, 0:N], ACT.Exp, bias=b.negmax[j][:],
                                     accum_out=b.z[j][:]).then_inc(slots[j]["terms"], 1)

            def kept(i, c):
                j = c % 2
                act.wait_ge(slots[j]["top8"], START + i + c // 2 + 1)
                nc.scalar.activation(b.e8[j][:], b.w8[j][:], ACT.Exp, bias=b.negmax[j][:]).then_inc(slots[j]["e8"], 1)

            def turned(i, c, groups):
                for k in groups:
                    x, y = k % 2, k % 4
                    act.wait_ge(tbank[x]["made"], START + 4 * (2 * i + c) + k // 2 + 1)
                    act.wait_ge(ring[y]["used"], START + 2 * (2 * i + c) + k // 4)
                    nc.scalar.activation(b.aT[y][:], b.tp[x][:], ACT.Copy).then_inc(ring[y]["filled"], 1)

            def values(i, c):
                act.wait_ge(ring[3]["used"], START + 2 * (2 * i + c) + 2)
                act.wait_ge(slots[c % 2]["out"], START + i + c // 2)
                nc.scalar.activation(b.osb[c % 2][:], b.o[:, 0:XW], ACT.Copy).then_inc(s["values_out"], 1)

            for c in range(2):
                query(0, c)
            for c in range(2):
                logits(0, c)
                terms(0, c)
            kept(0, 0)
            for c in range(2):
                sums(0, c)
            with act.Fori(0, PAIRS - 1) as i:
                for c in range(2):
                    query(i, c + 2)
                    logits(i, c + 2)
                    turned(i, c, range(6))
                    kept(i, c + 1)
                    turned(i, c, range(6, NG))
                    values(i, c)
                    terms(i, c + 2)
                    sums(i, c + 2)
            turned(PAIRS - 1, 0, range(2))
            kept(PAIRS - 1, 1)
            turned(PAIRS - 1, 0, range(2, NG))
            values(PAIRS - 1, 0)
            turned(PAIRS - 1, 1, range(NG))
            values(PAIRS - 1, 1)

        @block.vector
        def _(dve):
            st = Steps(dve, s["steps"])
            for j in range(2):
                st.mark(nc.vector.memset(b.l[j][:, N:], -BIG))

            def candidates(i, c):
                j = c % 2
                for n in range(NSEG):
                    at = n * SEG // LW
                    if n * SEG % LW == 0:
                        wait_apart(dve, lbank[at % 2]["read"], START + 2 * (2 * i + c) + at // 2 + 1, s["passed"])
                    last = nc.vector.max(b.lc[j][:, 8 * n:8 * n + 8], b.l[j][:, n * SEG:(n + 1) * SEG])
                    if n < NSEG - 1:
                        yield
                st.mark(last)
                yield

            def top(i, c):
                j = c % 2
                st.done(nc.vector.tensor_reduce(b.negmax[j][:], b.lc[j][:, 0:NC:8], AX.X, ALU.max, negate=True))
                nc.vector.tensor_reduce(b.hidden[j][:], b.lc[j][:, 7:NC:8], AX.X, ALU.max
                                        ).then_inc(slots[j]["cand"], 1)

            def search(i, c, ahead):
                j = c % 2
                use = i + c // 2
                small, run, kept, lowest = b.small[j], b.run[j], b.kept[j], b.lowest[j]

                def settle(fill=FILL, apart=False):
                    for _ in range(fill):
                        next(ahead, None)
                    if apart:
                        st.settle_apart(s["passed"])
                    else:
                        st.settle()

                st.mark(nc.vector.tensor_scalar(small[:, 0:1], b.negmax[j][:], -1.0, 0.25 - SPAN, ALU.mult, ALU.add))
                st.mark(nc.vector.scalar_tensor_tensor(out=small[:, 1:2], in0=b.negmax[j][:], scalar=-1.0,
                                                       in1=b.negmax[j][:], op0=ALU.mult, op1=ALU.max))
                settle(0)
                st.mark(nc.vector.scalar_tensor_tensor(out=b.cut[j][:], in0=small[:, 1:2], scalar=2.0 ** -22,
                                                       in1=small[:, 0:1], op0=ALU.mult, op1=ALU.add))
                dve.wait_ge(slots[j]["terms"], START + use + 1)
                st.mark(nc.vector.tensor_scalar(b.goal[j][:], b.z[j][:], TOP_P, None, ALU.mult))
                st.mark(nc.vector.tensor_scalar(b.least[j][:], b.z[j][:], MIN_SUM, None, ALU.mult))
                dve.wait_ge(slots[j]["ecand"], START + use + 1)
                settle(0)
                for k in range(halvings):
                    width = SPAN / 2 ** k
                    fill = FILL if k >= 2 else 0
                    st.mark(nc.vector.scalar_tensor_tensor(out=b.junk[:], in0=b.lc[j][:], scalar=b.cut[j][:],
                                                           in1=b.ec[j][:], op0=ALU.is_ge, op1=ALU.mult,
                                                           accum_out=b.mass[j][:]))
                    settle(fill)
                    st.mark(nc.vector.tensor_scalar(small[:, 0:1], b.mass[j][:], b.goal[j][:], width,
                                                    ALU.is_lt, ALU.mult))
                    settle(fill)
                    st.mark(nc.vector.scalar_tensor_tensor(
                        out=b.cut[j][:], in0=b.cut[j][:], scalar=width / 2 if k < halvings - 1 else width,
                        in1=small[:, 0:1], op0=ALU.add, op1=ALU.subtract))
                    settle(fill)
                st.mark(nc.vector.tensor_scalar(b.below[:], b.lc[j][:], b.cut[j][:], -BIG, ALU.is_ge, ALU.mult))
                st.mark(nc.vector.scalar_tensor_tensor(out=b.junk[:], in0=b.lc[j][:], scalar=b.cut[j][:],
                                                       in1=b.ec[j][:], op0=ALU.is_ge, op1=ALU.mult,
                                                       accum_out=run[:, 0:1]))
                settle()
                st.mark(nc.vector.tensor_tensor(b.below[:], b.below[:], b.lc[j][:], ALU.add))
                settle(apart=True)
                nc.vector.max(b.w8[j][:], b.below[:]).then_inc(slots[j]["top8"], 1)
                for _ in ahead:
                    pass
                dve.wait_ge(slots[j]["e8"], START + use + 1)
                st.mark(nc.vector.tensor_tensor_scan(run[:, 1:9], b.e8[j][:], b.zero8[:], run[:, 0:1], ALU.add, ALU.add))

            def finish(i, c, then):
                j = c % 2
                small, run, kept, lowest = b.small[j], b.run[j], b.kept[j], b.lowest[j]
                st.settle()
                st.mark(nc.vector.tensor_scalar(kept[:], run[:, 0:8], b.goal[j][:], 2 * BIG, ALU.is_lt, ALU.mult))
                st.mark(nc.vector.tensor_scalar(small[:, 2:3], run[:, 0:1], b.goal[j][:], None, ALU.is_ge))
                st.mark(nc.vector.tensor_scalar(small[:, 3:4], run[:, 8:9], b.goal[j][:], None, ALU.is_lt))
                st.settle()
                st.mark(nc.vector.tensor_scalar(lowest[:], kept[:], -1.0, BIG, ALU.mult, ALU.add))
                st.mark(nc.vector.tensor_scalar(kept[:], kept[:], -BIG, None, ALU.add))
                st.mark(nc.vector.tensor_tensor(small[:, 2:3], small[:, 2:3], small[:, 3:4], ALU.add))
                st.settle()
                st.mark(nc.vector.tensor_tensor(kept[:], kept[:], b.w8[j][:], ALU.min))
                st.mark(nc.vector.tensor_tensor(lowest[:], lowest[:], b.w8[j][:], ALU.max))
                then()
                st.settle()
                st.done(nc.vector.tensor_reduce(small[:, 3:4], lowest[:], AX.X, ALU.min))
                st.done(nc.vector.tensor_scalar(small[:, 3:4], small[:, 3:4], b.hidden[j][:], None, ALU.is_le))
                st.mark(nc.vector.tensor_tensor(g.unproved[:, bass.ds(2 * i + c, 1)], small[:, 2:3], small[:, 3:4], ALU.max))

            def mask(i, c):
                j = c % 2
                st.done(nc.vector.match_replace(b.l[j][:], b.kept[j][:], b.l[j][:], BIG))
                nc.vector.scalar_tensor_tensor(out=b.e[j][:], in0=b.l[j][:, 0:N], scalar=b.cut[j][:], in1=b.e[j][:],
                                               op0=ALU.is_ge, op1=ALU.mult).then_inc(slots[j]["mask"], 1)

            def outputs(i, c):
                j = c % 2
                dve.wait_ge(s["values_out"], START + 2 * i + c + 1)
                st.done(nc.vector.tensor_scalar(b.small[j][:, 4:5], b.least[j][:], b.osb[j][:, D:XW], None, ALU.max))
                st.done(nc.vector.reciprocal(b.small[j][:, 5:6], b.small[j][:, 4:5]))
                nc.vector.tensor_scalar(xa_new[:, bass.ds(2 * i + c, 1), 0:D].rearrange("p o d -> p (o d)"),
                                        b.osb[j][:, 0:D], b.small[j][:, 5:6], None, ALU.mult).then_inc(slots[j]["out"], 1)

            def nothing():
                pass

            for j in range(2):
                nc.vector.memset(b.qt[j][DA:P], 0.0).then_inc(s["padded"], 1)
            st.done(nc.vector.memset(b.zero8[:], 0.0))
            for c in range(2):
                for _ in candidates(0, c):
                    pass
                st.settle()
                top(0, c)
            search(0, 0, iter(()))
            finish(0, 0, nothing)
            mask(0, 0)
            with dve.Fori(0, PAIRS - 1) as i:
                st.loop(i, 2 * (25 + 3 * halvings))
                for c in range(2):
                    search(i, c + 1, candidates(i, c + 2))
                    finish(i, c + 1, lambda: top(i, c + 2))
                    mask(i, c + 1)
                    outputs(i, c)
            st.leave(PAIRS - 1)
            search(PAIRS - 1, 1, iter(()))
            finish(PAIRS - 1, 1, nothing)
            mask(PAIRS - 1, 1)
            for c in range(2):
                outputs(PAIRS - 1, c)


def places(nc, used, g, step, buf):
    s = sems(nc, used, f"pl{step}", "pe steps")
    with ExitStack() as mem:
        tot = mem.enter_context(nc.sbuf_tensor(f"pl{step}_tot", [P, T], F32))
        run = mem.enter_context(nc.sbuf_tensor(f"pl{step}_run", [P, T], F32))
        far = mem.enter_context(nc.sbuf_tensor(f"pl{step}_far", [P, T], F32))
        edge = mem.enter_context(nc.sbuf_tensor(f"pl{step}_edge", [P, T], F32))
        cnt = mem.enter_context(nc.sbuf_tensor(f"pl{step}_cnt", [P, 1], F32))
        pp = buf.racc[:, 0:2 * T].rearrange("p (k t) -> p k t", k=2)
        with nc.Block() as block:
            @block.tensor
            def _(pe):
                nc.tensor.matmul(pp[:, 0, :], g.ones[:], g.unproved[:], start=True, stop=True)
                nc.tensor.matmul(pp[:, 1, :], g.tri[:], g.unproved[:], start=True, stop=True).then_inc(s["pe"], 1)

            @block.vector
            def _(dve):
                st = Steps(dve, s["steps"])
                st.mark(nc.vector.memset(edge[:], 0.0))
                st.mark(nc.vector.tensor_scalar(far[:], g.unproved[:], -2.0 * N, 2.0 * N, ALU.mult, ALU.add))
                dve.wait_ge(s["pe"], START + 1)
                st.done(nc.vector.tensor_copy(tot[:], pp[:, 0, :]))
                st.done(nc.vector.tensor_tensor_scan(run[:], tot[:], edge[:], 0.0, ALU.add, ALU.add))
                st.mark(nc.vector.tensor_tensor(far[:], far[:], run[:], ALU.add))
                st.mark(nc.vector.tensor_scalar(edge[:], g.iota[:, 0:T], float(P), None, ALU.mult))
                st.settle()
                st.mark(nc.vector.tensor_tensor(far[:], far[:], tot[:], ALU.subtract))
                st.done(nc.vector.tensor_scalar(edge[:], edge[:], run[:, T - 1:T], None, ALU.is_lt, ALU.add,
                                                accum_out=cnt[:]))
                st.mark(nc.vector.tensor_tensor(g.place[:], far[:], pp[:, 1, :], ALU.add))
                st.done(nc.vector.tensor_copy(g.groups[:], cnt[:]))


def rest(nc, used, g, step, buf):
    s = sems(nc, used, f"re{step}", "picked pe xg w1g qg l0 l1 lr0 lr1 max terms aT tp sel steps mask out turn ap fill add passed")
    xa, xa_new = g.xa[step % 2], g.xa[(step + 1) % 2]
    b = buf
    l, e, sel, junk = b.l[0][:, 0:N], b.e[0], b.e[1], b.l[1][:, 0:N]
    NG = T // CH

    def groups(eng, body):
        count = eng.value_load(g.groups[0:1, 0:1], min_val=0, max_val=T)
        with eng.If(count > 0):
            with eng.Fori(0, count) as n:
                body(n)
            eng.nop()
        with eng.Else():
            eng.nop()

    with nc.Block() as block:
        @block.tensor
        def _(pe):
            def body(n):
                pe.wait_ge(s["picked"], START + n + 1)
                for t in range(T):
                    last = nc.tensor.matmul(b.tp[0][:, 0, :], xa[:, t, 0:D], sel[:, t * P:(t + 1) * P],
                                            start=(t == 0), stop=(t == T - 1))
                last.then_inc(s["pe"], 1)
                pe.wait_ge(s["xg"], START + n + 1)
                nc.tensor.matmul(b.tp[1][0:DA, 0, :], g.W1T[:], b.xg[:], start=True, stop=True).then_inc(s["pe"], 1)
                wait_apart(pe, s["w1g"], START + n + 1, s["passed"])
                nc.tensor.matmul(b.tp[0][0:DA, 0, :], g.W2T[:], b.w1g[:], start=True, stop=True).then_inc(s["pe"], 1)
                pe.wait_ge(s["qg"], START + n + 1)
                for c in range(NL):
                    pe.wait_ge((s["lr0"], s["lr1"])[c % 2], START + 2 * n + c // 2)
                    for k in range(LW // CW):
                        cols = slice(c * LW + k * CW, c * LW + (k + 1) * CW)
                        last = nc.tensor.matmul(b.lp[c % 2][:, k, :], b.qt[0][:], g.qkT[:, cols], start=True, stop=True)
                    last.then_inc((s["l0"], s["l1"])[c % 2], 1)
                pe.wait_ge(s["mask"], START + n + 1)
                for k in range(NG):
                    pe.wait_ge(s["aT"], START + NG * n + k)
                    for c in range(CH):
                        m = CH * k + c
                        last = nc.tensor.transpose(b.tp[0][:, c, :], e[:, m * P:(m + 1) * P], g.ident[:])
                    last.then_inc(s["tp"], 1)
                    pe.wait_ge(s["aT"], START + NG * n + k + 1)
                    for c in range(CH):
                        m = CH * k + c
                        last = nc.tensor.matmul(b.o[:, 0:XW], b.aT[0][:, c, :], xa[:, m, :], start=(m == 0),
                                                stop=(m == T - 1))
                    last.then_inc(s["ap"], 1)
                pe.wait_ge(s["out"], START + n + 1)
                for k in range(NG):
                    pe.wait_ge(s["fill"], START + NG * n + k)
                    for c in range(CH):
                        m = CH * k + c
                        last = nc.tensor.transpose(b.tp[0][:, c, :], sel[:, m * P:(m + 1) * P], g.ident[:])
                    last.then_inc(s["turn"], 1)
                    pe.wait_ge(s["fill"], START + NG * n + k + 1)
                    pe.wait_ge(s["add"], START + NG * n + k)
                    for c in range(CH):
                        last = nc.tensor.matmul(b.tp[1][:, c, :], b.aT[0][:, c, :], b.xg[:], start=True, stop=True)
                    last.then_inc(s["sel"], 1)

            groups(pe, body)

        @block.scalar
        def _(act):
            def body(n):
                act.wait_ge(s["pe"], START + 3 * n + 1)
                act.wait_ge(s["sel"], START + NG * n)
                nc.scalar.activation(b.xg[:], b.tp[0][:, 0, :], ACT.Copy).then_inc(s["xg"], 1)
                act.wait_ge(s["pe"], START + 3 * n + 2)
                nc.scalar.activation(b.w1g[:], b.tp[1][0:DA, 0, :], ACT.Copy).then_inc(s["w1g"], 1)
                act.wait_ge(s["pe"], START + 3 * n + 3)
                nc.scalar.activation(b.qt[0][0:DA], b.tp[0][0:DA, 0, :], ACT.Copy).then_inc(s["qg"], 1)
                for c in range(NL):
                    act.wait_ge((s["l0"], s["l1"])[c % 2], START + 2 * n + c // 2 + 1)
                    nc.scalar.activation(l[:, c * LW:(c + 1) * LW], b.lp[c % 2][:].rearrange("p k n -> p (k n)"), ACT.Copy
                                         ).then_inc((s["lr0"], s["lr1"])[c % 2], 1)
                act.wait_ge(s["max"], START + n + 1)
                nc.scalar.activation(e[:], l, ACT.Exp, bias=b.negmax[0][:], accum_out=b.z[0][:]).then_inc(s["terms"], 1)
                for k in range(NG):
                    act.wait_ge(s["tp"], START + NG * n + k + 1)
                    act.wait_ge(s["ap"], START + NG * n + k)
                    nc.scalar.activation(b.aT[0][:], b.tp[0][:], ACT.Copy).then_inc(s["aT"], 1)
                for k in range(NG):
                    act.wait_ge(s["turn"], START + NG * n + k + 1)
                    act.wait_ge(s["sel"], START + NG * n + k)
                    act.wait_ge(s["ap"], START + NG * n + NG)
                    nc.scalar.activation(b.aT[0][:], b.tp[0][:], ACT.Copy).then_inc(s["fill"], 1)

            groups(act, body)

        @block.vector
        def _(dve):
            st = Steps(dve, s["steps"])

            def body(n):
                st.loop(n, 21 + 6 * SLOW_STEPS + T - NG)
                lo, hi, cut, mass, goal = b.cut[0], b.cut[1], b.mass[0], b.mass[1], b.goal[0]
                small, least, room = b.small[0], b.least[0], b.goal[1]
                for t in range(T):
                    last = nc.vector.tensor_scalar(sel[:, t * P:(t + 1) * P], g.iota[:], g.place[:, t:t + 1], None,
                                                   ALU.is_equal)
                last.then_inc(s["picked"], 1)
                st.mark(nc.vector.tensor_scalar(b.away[:], g.place[:], 0.0, None, ALU.is_lt))
                st.mark(nc.vector.tensor_scalar(b.off[:], g.place[:], float(P), None, ALU.is_ge))
                st.settle()
                st.done(nc.vector.tensor_tensor(b.away[:], b.away[:], b.off[:], ALU.add))
                for x in range(2):
                    dve.wait_ge((s["lr0"], s["lr1"])[x], START + 2 * n + 2)
                nc.vector.tensor_reduce(b.negmax[0][:], l, AX.X, ALU.max, negate=True).then_inc(s["max"], 1)
                dve.wait_ge(s["max"], START + n + 1)
                st.mark(nc.vector.tensor_scalar(small[:, 0:1], b.negmax[0][:], -1.0, 0.25, ALU.mult, ALU.add))
                st.mark(nc.vector.scalar_tensor_tensor(out=small[:, 1:2], in0=b.negmax[0][:], scalar=-1.0,
                                                       in1=b.negmax[0][:], op0=ALU.mult, op1=ALU.max))
                st.settle()
                st.done(nc.vector.scalar_tensor_tensor(out=hi[:], in0=small[:, 1:2], scalar=2.0 ** -22,
                                                       in1=small[:, 0:1], op0=ALU.mult, op1=ALU.add))
                st.mark(nc.vector.tensor_scalar(lo[:], hi[:], -2.0 * SPAN, None, ALU.add))
                dve.wait_ge(s["terms"], START + n + 1)
                st.mark(nc.vector.tensor_scalar(goal[:], b.z[0][:], TOP_P, None, ALU.mult))
                st.mark(nc.vector.tensor_scalar(least[:], b.z[0][:], MIN_SUM, None, ALU.mult))
                st.settle()
                st.done(nc.vector.tensor_scalar(small[:, 2:3], lo[:], hi[:], 0.5, ALU.add, ALU.mult))
                for k in range(SLOW_STEPS):
                    st.done(nc.vector.scalar_tensor_tensor(out=junk, in0=l, scalar=small[:, 2:3], in1=e[:],
                                                           op0=ALU.is_ge, op1=ALU.mult, accum_out=mass[:]))
                    st.mark(nc.vector.tensor_scalar(b.flag[:, 0:1], mass[:], goal[:], None, ALU.is_lt))
                    st.mark(nc.vector.tensor_scalar(b.flag[:, 1:2], mass[:], goal[:], None, ALU.is_ge))
                    st.settle_apart(s["passed"])
                    st.mark(nc.vector.copy_predicated(hi[:], b.flag[:, 0:1], small[:, 2:3]))
                    st.mark(nc.vector.copy_predicated(lo[:], b.flag[:, 1:2], small[:, 2:3]))
                    st.settle()
                    st.done(nc.vector.tensor_scalar(small[:, 2:3], lo[:], hi[:], 0.5, ALU.add, ALU.mult))
                st.done(nc.vector.scalar_tensor_tensor(out=junk, in0=l, scalar=hi[:], in1=e[:], op0=ALU.is_ge,
                                                       op1=ALU.mult, accum_out=mass[:]))
                st.mark(nc.vector.tensor_tensor(room[:], goal[:], mass[:], ALU.subtract))
                st.mark(nc.vector.scalar_tensor_tensor(out=junk, in0=l, scalar=hi[:], in1=e[:], op0=ALU.is_lt, op1=ALU.mult))
                st.settle()
                st.mark(nc.vector.scalar_tensor_tensor(out=junk, in0=l, scalar=lo[:], in1=junk, op0=ALU.is_ge, op1=ALU.mult))
                st.mark(nc.vector.scalar_tensor_tensor(out=e[:], in0=l, scalar=hi[:], in1=e[:], op0=ALU.is_ge, op1=ALU.mult))
                st.settle()
                st.done(nc.vector.tensor_tensor_scan(l, junk, junk, 0.0, ALU.add, ALU.max))
                st.done(nc.vector.tensor_tensor(l, l, junk, ALU.subtract))
                st.done(nc.vector.scalar_tensor_tensor(out=l, in0=l, scalar=room[:], in1=junk, op0=ALU.is_lt, op1=ALU.mult))
                nc.vector.tensor_tensor(e[:], e[:], l, ALU.add).then_inc(s["mask"], 1)
                dve.wait_ge(s["ap"], START + NG * n + NG)
                st.done(nc.vector.tensor_scalar(small[:, 4:5], least[:], b.o[:, D:XW], None, ALU.max))
                st.done(nc.vector.reciprocal(small[:, 5:6], small[:, 4:5]))
                nc.vector.tensor_scalar(b.xg[:], b.o[:, 0:D], small[:, 5:6], None, ALU.mult).then_inc(s["out"], 1)
                for k in range(NG):
                    dve.wait_ge(s["sel"], START + NG * n + k + 1)
                    for c in range(CH):
                        t = CH * k + c
                        last = nc.vector.scalar_tensor_tensor(out=xa_new[:, t, 0:D], in0=xa_new[:, t, 0:D],
                                                              scalar=b.away[:, t:t + 1], in1=b.tp[1][:, c, :],
                                                              op0=ALU.mult, op1=ALU.add)
                        st.mark(last) if c < CH - 1 else last.then_inc(s["add"], 1)
                st.settle()
                dve.wait_ge(s["add"], START + NG * n + NG)
                st.done(nc.vector.tensor_scalar(g.place[:], g.place[:], -float(P), None, ALU.add))
                assert st.n == st.per, st.n

            groups(dve, body)


def last_norms(nc, used, g, io, h):
    s = sems(nc, used, "n2", "loaded steps stds stored")
    with ExitStack() as mem:
        x1 = mem.enter_context(nc.sbuf_tensor("n2_x1", [P, T, D], F32))
        w = mem.enter_context(nc.sbuf_tensor("n2_w", [P, T, D], F32))
        stat = mem.enter_context(nc.sbuf_tensor("n2_stat", [P, 2, T], F32))
        with nc.Block() as block:
            @block.sync
            def _(sp):
                sp.dma_start(x1[:], g.x1_dram.rearrange("(t p) d -> p t d", p=P)).then_inc(s["loaded"], 16)
                sp.wait_ge(s["steps"], START + 19)
                sp.dma_start(io["out"].rearrange("(t p) d -> p t d", p=P), h[:]).then_inc(s["stored"], 16)
                sp.wait_ge(s["stored"], START + 16)

            @block.vector
            def _(dve):
                st = Steps(dve, s["steps"])
                norm_before(st, nc, h[:], h[:], w[:], stat)
                dve.wait_ge(s["stds"], START + 1)
                norm_after(st, nc, h[:], h[:], stat)
                st.done(nc.vector.tensor_tensor(h[:], h[:], g.gb[:, 0:1, :].broadcast_to([P, T, D]), ALU.mult))
                st.done(nc.vector.tensor_tensor(h[:], h[:], g.gb[:, 1:2, :].broadcast_to([P, T, D]), ALU.add))
                dve.wait_ge(s["loaded"], START + 16)
                st.done(nc.vector.tensor_tensor(h[:], h[:], x1[:], ALU.add))
                norm_before(st, nc, h[:], h[:], w[:], stat)
                dve.wait_ge(s["stds"], START + 2)
                norm_after(st, nc, h[:], h[:], stat)
                assert st.n == 19

            @block.scalar
            def _(act):
                for k, steps in enumerate((6, 17)):
                    act.wait_ge(s["steps"], START + steps)
                    nc.scalar.activation(stat[:, 1, :], stat[:, 0, :], ACT.Sqrt).then_inc(s["stds"], 1)


def program(nc, io):
    g = Names()
    with ExitStack() as keep:
        def sb(name, shape, dt=F32):
            return keep.enter_context(nc.sbuf_tensor(name, shape, dt))

        g.adjT = nc.dram_tensor("adjT_store", (T, P, N), BF16).ap()
        g.sl_dram = nc.dram_tensor("sl_store", (HEADS, N), F32).ap()
        g.h_dram = nc.dram_tensor("h_store", (N, D), F32).ap()
        g.x1_dram = nc.dram_tensor("x1_store", (N, D), F32).ap()
        g.ident, g.ones, g.tri, g.iota = (sb(n, [P, P]) for n in ("ident", "ones", "tri", "iota"))
        g.W1T, g.W3T, g.W2T = sb("W1T", [P, DA]), sb("W3T", [P, DA]), sb("W2T", [DA, DA])
        g.UT, g.gb = sb("UT", [P, 2 * STEPS, D]), sb("gb", [P, 2, D])
        with ExitStack() as early:
            def eb(name, shape, dt=F32):
                return early.enter_context(nc.sbuf_tensor(name, shape, dt))

            g.WhA, g.gsum = eb("WhA", [P, T, AC]), eb("gsum", [P, T, AC])
            g.sl, g.sr, g.nsr, g.E1, g.E2, g.selfp = (eb(n, [P, T, HEADS]) for n in ("sl", "sr", "nsr", "E1", "E2", "selfp"))
            g.diag = eb("diag", [P, T, 1])
            phase(nc, setup, g, io)
            with ExitStack() as mem:
                slb = mem.enter_context(nc.sbuf_tensor("slb", [P, HEADS, N], F32))
                G = mem.enter_context(nc.sbuf_tensor("G", [P, T, PARTS, GC], BF16))
                phase(nc, tables, g, io, G, slb)
                phase(nc, gat, g, io, G, slb)
            phase(nc, first_norm, g, io)
        g.xf = sb("xf", [P, T, D])
        g.xs = sb("xs", [P, T, SW], BF16)
        g.xa = [sb(f"xa{k}", [P, T, XW]) for k in range(2)]
        phase(nc, place_x1, g)
        g.qkT = sb("qkT", [P, N])
        g.unproved, g.place, g.rsum, g.groups = sb("unproved", [P, T]), sb("place", [P, T]), sb("rsum", [P, T]), sb("groups", [P, 1], I32)
        for step in range(STEPS):
            with ExitStack() as mem:
                h = mem.enter_context(nc.sbuf_tensor(f"h{step}", [P, T, D], F32)) if step else None
                phase(nc, project, g, step, h)
            with ExitStack() as mem:
                def tb(name, shape, dt=F32):
                    return mem.enter_context(nc.sbuf_tensor(f"s{step}_{name}", shape, dt))

                def pair(name, shape, dt=F32):
                    return [tb(f"{name}{j}", shape, dt) for j in range(2)]

                def ps(name, shape):
                    return mem.enter_context(nc.psum_tensor(f"s{step}_{name}", shape, F32))

                b = Names()
                b.l, b.e = pair("l", [P, N + 8]), pair("e", [P, N])
                b.rt = pair("rt", [P, T, P], BF16)
                b.rsums, b.qt = pair("rsums", [P, SW]), pair("qt", [P, P])
                b.lc, b.ec, b.junk, b.below = pair("lc", [P, NC]), pair("ec", [P, NC]), tb("junk", [P, NC]), tb("below", [P, NC])
                b.negmax, b.hidden, b.cut, b.mass, b.goal, b.z, b.least = (
                    pair(name, [P, 1]) for name in ("negmax", "hidden", "cut", "mass", "goal", "z", "least"))
                b.w8, b.e8, b.kept, b.lowest = (pair(n, [P, 8]) for n in ("w8", "e8", "kept", "lowest"))
                b.run, b.small = pair("run", [P, 9]), pair("small", [P, 6])
                b.zero8, b.flag = tb("zero8", [P, 8]), tb("flag", [P, 2], I32)
                b.aT = [tb(f"aT{y}", [P, CH, P]) for y in range(4)]
                b.lp = [ps(f"lp{x}", [P, LW // CW, CW]) for x in range(2)]
                b.tp = [ps(f"tp{x}", [P, CH, P]) for x in range(2)]
                b.racc, b.o = ps("racc", [P, CW]), ps("o", [P, CW])
                b.osb = pair("osb", [P, XW])
                b.xg, b.w1g, b.away, b.off = tb("xg", [P, P]), tb("w1g", [DA, P]), tb("away", [P, T]), tb("off", [P, T])
                phase(nc, attend, g, step, b)
                phase(nc, places, g, step, b)
                phase(nc, rest, g, step, b)
        h = sb("h_last", [P, T, D])
        phase(nc, project, g, STEPS, h)
        phase(nc, last_norms, g, io, h)


_INS = ["x", "adj", "L0_gnn_W", "L0_gnn_a_l", "L0_gnn_a_r", "L1_gnn_W1", "L1_gnn_W2", "L1_gnn_W3", "L1_gnn_U1",
        "L1_gnn_U2", "L1_gnn_ln_g", "L1_gnn_ln_b"]


def build(nc, **args):
    program(nc, {name.split("_gnn_")[-1]: ap for name, ap in args.items()})


def kernel(**inputs):
    from concourse import bacc
    from concourse.bass_utils import run_bass_kernel_spmd

    nc = bacc.Bacc("TRN2", target_bir_lowering=False, num_devices=1)
    arrays, args = {}, {}
    for name in _INS:
        a = np.ascontiguousarray(inputs[name])
        arrays[name] = a
        args[name] = nc.dram_tensor(name, a.shape, mybir.dt.from_np(a.dtype), kind="ExternalInput").ap()
    args["out"] = nc.dram_tensor("out", (N, D), F32, kind="ExternalOutput").ap()
    build(nc, **args)
    r = run_bass_kernel_spmd(nc, [arrays], core_ids=[0])
    return r.results[0]["out"]
```
